# Optimizing a Trainium2 kernel written in Bass

```python
import numpy as np
import jax
import jax.numpy as jnp

def _softmax(x, axis=-1):
    return jax.nn.softmax(x, axis=axis)

def _gelu(x):
    return jax.nn.gelu(x, approximate=True)

def _silu(x):
    return jax.nn.silu(x)

def _sigmoid(x):
    return jax.nn.sigmoid(x)

def _layernorm(x, axis=-1, eps=1e-05):
    m = jnp.mean(x, axis=axis, keepdims=True)
    v = jnp.var(x, axis=axis, keepdims=True)
    return (x - m) / jnp.sqrt(v + eps)

def _scatter_add(tgt, idx, src, axis=0):
    return tgt.at[idx].add(src)

def _segment_sum(src, seg, n):
    return jax.ops.segment_sum(src, seg, n)
kernel_name = 'mk_adj_preln_d2_adj_r2_14fe14'

def setup_inputs(seed: int=0):
    np.random.seed(seed)
    _w = jnp.asarray

    def _rec_inputs():
        import jax
        import jax.numpy as jnp
        _gk = jax.random.key(seed)
        x = 7.22e-05 + 1 * jax.random.normal(jax.random.fold_in(_gk, 1), (8, 2048, 128), jnp.float32)
        _a = jax.random.bernoulli(jax.random.fold_in(_gk, 2), 0.0078125, (2048, 2048))
        _a = jnp.logical_or(_a, jnp.swapaxes(_a, -1, -2))
        _a = jnp.logical_or(_a, jnp.eye(2048, dtype=bool))
        _af = _a.astype(jnp.float32)
        _af = _af * jax.random.uniform(jax.random.fold_in(_gk, 3), (2048, 2048), jnp.float32, 0.05, 0.119748)
        adj = _af
        return (x, adj)
    x, adj = _rec_inputs()

    def _L0_gnn_setup():
        import jax, jax.numpy as jnp
        import numpy as np
        B, N, F_IN, F_OUT = (8, 2048, 128, 128)
        key = jax.random.key(seed)
        k1, k2, k3 = jax.random.split(key, 3)
        H = jax.random.normal(k1, (B, N, F_IN), dtype=jnp.float32)
        W = jax.random.normal(k2, (F_IN, F_OUT), dtype=jnp.float32) * (1.0 / np.sqrt(F_IN))
        A = jax.random.normal(k3, (N, N), dtype=jnp.float32) * (1.414 * np.sqrt(2.0 / (N + N)))
        return {'H': H, 'W': W, 'A': A}
    _L0_gnn_all = _L0_gnn_setup()
    _L0_gnn_in = {k: v for k, v in _L0_gnn_all.items() if k in ('W',)}
    del _L0_gnn_all

    def _L1_gnn_setup():
        import jax, jax.numpy as jnp
        import numpy as np
        B, J, F_IN, F_OUT = (8192, 17, 128, 128)
        key = jax.random.key(seed)
        k1, k2, k3, k4 = jax.random.split(key, 4)
        gain = 1.414
        bound = gain * np.sqrt(6.0 / (F_IN + F_OUT))
        W = jax.random.uniform(k2, (3, F_IN, F_OUT), dtype=jnp.float32, minval=-bound, maxval=bound)
        stdv = 1.0 / np.sqrt(F_OUT)
        bias = jax.random.uniform(k4, (F_OUT,), dtype=jnp.float32, minval=-stdv, maxval=stdv)
        return {'x': jax.random.normal(k1, (B, J, F_IN), dtype=jnp.float32), 'W': W, 'adj': jax.random.uniform(k3, (J, J), dtype=jnp.float32), 'bias': bias}
    _L1_gnn_all = _L1_gnn_setup()
    _L1_gnn_in = {k: v for k, v in _L1_gnn_all.items() if k in ('W', 'bias')}
    del _L1_gnn_all
    return {'x': x, 'adj': adj, 'L0_gnn_W': _L0_gnn_in['W'], 'L1_gnn_W': _L1_gnn_in['W'], 'L1_gnn_bias': _L1_gnn_in['bias']}

def reference(x, adj, L0_gnn_W, L1_gnn_W, L1_gnn_bias):
    import jax
    import jax.numpy as jnp

    def _L0_gnn_ref(H, W, A):
        import jax, jax.numpy as jnp
        import numpy as np
        B, N, F_IN, F_OUT = (8, 2048, 128, 128)
        HW = jnp.einsum('bnf,fo->bno', H, W)
        A_norm = jax.nn.relu((A + A.T) * 0.5)
        D = jnp.sum(A_norm, axis=1)
        D_safe = jnp.where(D > 0, D, 1.0)
        d_inv_sqrt = jnp.where(D > 0, D_safe ** (-0.5), 0.0)
        DAD = d_inv_sqrt[:, None] * A_norm * d_inv_sqrt[None, :]
        L_norm = jnp.eye(N, dtype=H.dtype) - DAD
        out = jnp.einsum('nm,bmo->bno', L_norm, HW)
        return jax.nn.relu(out)

    def _L1_gnn_ref(x, W, adj, bias):
        import jax, jax.numpy as jnp
        import numpy as np
        B, J, F_IN, F_OUT = (8192, 17, 128, 128)
        adj_0 = jnp.diag(jnp.diagonal(adj))
        adj_1 = jnp.triu(adj, k=1)
        adj_2 = jnp.tril(adj, k=-1)
        h = jnp.einsum('bjf,kfo->kbjo', x, W)
        out = jnp.einsum('ij,bjo->bio', adj_0, h[0]) + jnp.einsum('ij,bjo->bio', adj_1, h[1]) + jnp.einsum('ij,bjo->bio', adj_2, h[2])
        return out + bias[None, None, :]
    h = jnp.maximum(_layernorm(x, axis=-1), 0.0)
    x = x + _L0_gnn_ref(h, L0_gnn_W, adj)
    h = jnp.maximum(_layernorm(x, axis=-1), 0.0)
    x = x + _L1_gnn_ref(h, L1_gnn_W, adj, L1_gnn_bias)
    return x

_drawn_inputs = setup_inputs


def setup_inputs(seed=0):
    import zlib

    import numpy as np

    out = dict(_drawn_inputs(seed))
    spreads = {}
    factors = {}
    for name, (base, spread) in spreads.items():
        noise = np.random.default_rng([zlib.crc32(name.encode()), seed]).standard_normal(out[name].shape)
        drawn = base * np.exp(spread * noise) if base else spread * noise
        out[name] = jnp.asarray(drawn.astype(out[name].dtype))
    for name, factor in factors.items():
        out[name] = (out[name] * factor).astype(out[name].dtype)
    return out
```

```python
import numpy as np
from contextlib import ExitStack

import concourse.bass as bass
from concourse import mybir

F32 = mybir.dt.float32
F32R = mybir.dt.float32r
ALU = mybir.AluOpType
ACT = mybir.ActivationFunctionType
AX = mybir.AxisListType

P = 128
B, N, F = 8, 2048, 128
NB = N // P
HB = B // 2
W = HB * F
NQ = 4
Q = N // NQ
EPS = 1e-5
L1 = 2 * NB
LAST = 4 * NB


class Step:

    def __init__(self, i, c):
        self.i, self.c = i, c

    def of(self, mul, add):
        return mul * self.c + add if self.i is None else self.i * (2 * mul) + (mul * self.c + add)

    def pair(self, shift, mul):
        k = mul * ((self.c + shift) // 2)
        return k if self.i is None else self.i * mul + k


def wait(eng, sem, value):
    if isinstance(value, int) and value <= 0:
        return
    eng.wait_ge(sem, value)


def run_steps(eng, body):
    def loop(first, last):
        with eng.Fori(0, (last - first) // 2) as i:
            for c in (first, first + 1):
                body(Step(i, c))

    def single(*steps):
        for c in steps:
            body(Step(None, c))

    single(0, 1, 2, 3)
    loop(4, 14)
    single(14, 15, 16, 17)
    loop(18, 30)
    single(30, 31, 32, 33)
    loop(34, 46)
    single(46, 47, 48, 49)
    loop(50, 62)
    single(62, 63)


def build(nc, x, adj, w_l0, w_l1, bias, out):
    s_dram = nc.dram_tensor("s_dram", (NB, P, N), F32, kind="Internal").ap()
    at_dram = nc.dram_tensor("at_dram", (NB, P, N + P), F32, kind="Internal").ap()
    t_dram = nc.dram_tensor("t_dram", (L1, P, W), F32, kind="Internal").ap()
    g_dram = nc.dram_tensor("g_dram", (L1, P, 2 * W), F32, kind="Internal").ap()

    xv = x.rearrange("(h b) (n p) f -> h n p b f", b=HB, p=P)
    ov = out.rearrange("(h b) (n p) f -> h n p b f", b=HB, p=P)
    rows_v = adj.rearrange("(n p) m -> n p m", p=P)
    cols_v = adj.rearrange("(j p) (n c) -> n p j c", p=P, c=P)

    ctx = ExitStack()
    with ctx:
        def sb(name, shape, dt=F32, at=ctx):
            return at.enter_context(nc.sbuf_tensor(name, shape, dt))

        def sems(*names):
            return [ctx.enter_context(nc.semaphore(n)) for n in names]

        def many(name, n):
            return [ctx.enter_context(nc.semaphore(f"{name}{k}")) for k in range(n)]

        class Norm:
            def __init__(self, n, at=ctx):
                self.st, self.mv = sb(n + "_st", [P, HB, 6], at=at), sb(n + "_mv", [P, HB, 2], at=at)
                self.ve, self.rs, self.nm = (sb(n + k, [P, HB], at=at) for k in ("_ve", "_rs", "_nm"))

        Xh = sb("Xh", [P, NB, W], F32R)
        with ExitStack() as early:
            hst = sb("hst", [P, NB, W], at=early)
            rowb = sb("rowb", [P, 3, N], at=early)
            colb = sb("colb", [P, 3, N], at=early)
            sring = sb("sring", [P, 4, 4 * P], at=early)
            drow = sb("drow", [P, NB, NQ], at=early)
            n0 = Norm("n0", early)
        Xl = sb("Xl", [P, NB, W], F32R)
        Yh = sb("Yh", [P, NB, W], F32R)
        Yl = sb("Yl", [P, NB, W], F32R)
        Lh = sb("Lh", [P, NQ, Q], F32R)
        Ll = sb("Ll", [P, NQ, Q], F32R)
        C = sb("C", [P, NQ, Q])
        R = sb("R", [P, NQ, Q])
        AT = sb("AT", [P, 2, N + P])
        zTh, zTl = sb("zTh", [P, W], F32R), sb("zTl", [P, W], F32R)
        hTh, hTl = sb("hTh", [P, W], F32R), sb("hTl", [P, W], F32R)
        z = sb("z", [P, W])
        x1 = sb("x1", [P, 2, W])
        xe = sb("xe", [P, W])
        xp = sb("xp", [P, W])
        g12 = sb("g12", [P, 2, W])
        Wh, Wl = sb("Wh", [P, 4 * F], F32R), sb("Wl", [P, 4 * F], F32R)
        biasb = sb("biasb", [P, F])
        ident = sb("ident", [P, P])
        dmid = sb("dmid", [P, P])
        dup = sb("dup", [P, P])
        lx = dmid
        lxh, lxl = sb("lxh", [P, P], F32R), sb("lxl", [P, P], F32R)
        scal = sb("scal", [P, 4, NB])
        cur_e, cur_g, cur_p = sb("cur_e", [P, 4]), sb("cur_g", [P, 4]), sb("cur_p", [P, 4])
        ones = sb("ones", [P, 1])
        tiny = sb("tiny", [P, 1])
        mhalf, half = sb("mhalf", [P, NB]), sb("half", [P, NB])
        d1, d2 = sb("d1", [P, NB]), sb("d2", [P, NB])
        dsafe = sb("dsafe", [P, NB])

        ne, npn = Norm("ne"), Norm("np")

        psAcc = ctx.enter_context(nc.psum_tensor("psAcc", [P, 2, W], F32))
        psA = ctx.enter_context(nc.psum_tensor("psA", [P, 2, 4 * P], F32))
        psZ = ctx.enter_context(nc.psum_tensor("psZ", [P, W], F32))
        psW = ctx.enter_context(nc.psum_tensor("psW", [P, W], F32))
        psG = ctx.enter_context(nc.psum_tensor("psG", [P, 2, 512], F32))
        psD = psW[:, 0:NB * NB].rearrange("p (j k) -> p j k", k=NB)

        ld_row, ld_col = many("ld_row", 3), many("ld_col", 3)
        ld_x0 = many("ld_x0_", NB)
        ld_c, ld_r, st_s = many("ld_c", NQ), many("ld_r", NQ), many("st_s", NQ)
        st_at, st_t, ld_t, st_o = many("st_at", 2), many("st_t", 2), many("ld_t", 2), many("st_o", 2)
        ld_w, ld_diag, ld_bias, ld_xe, ld_xp, st_g, ld_g2, ld_lx = sems(
            "ld_w", "ld_diag", "ld_bias", "ld_xe", "ld_xp", "st_g", "ld_g2", "ld_lx")
        const0, ident_ok, whi_ok, wlo_ok, d_zero = sems("const0", "ident_ok", "whi_ok", "wlo_ok", "d_zero")
        p0T, p0S, p0R, p0D = sems("p0T", "p0S", "p0R", "p0D")
        s0_st, s0_mv, s0_ve, s0_rs, s0_nm, s0_h = sems("s0_st", "s0_mv", "s0_ve", "s0_rs", "s0_nm", "s0_h")
        d_sums, d_sum, d_none, d_safe, d_inv, d_sq, d_ok = sems(
            "d_sums", "d_sum", "d_none", "d_safe", "d_inv", "d_sq", "d_ok")
        rT, S_ok, at_ok, lhi, llo, used = sems("rT", "S_ok", "at_ok", "lhi", "llo", "used")
        mk_c, mk_s, mk_ok = sems("mk_c", "mk_s", "mk_ok")
        prep_hi, prep_lo = sems("prep_hi", "prep_lo")
        cur0, = sems("cur0")
        cur_ok, hsum, z_ok, zT, zThi, zTlo, w_ok, r1_ok, x1_ok = sems(
            "cur_ok", "hsum", "z_ok", "zT", "zThi", "zTlo", "w_ok", "r1_ok", "x1_ok")
        e_st, e_mv, e_ve, e_rs, e_nm, h2_ok, hT, hThi, hTlo = sems(
            "e_st", "e_mv", "e_ve", "e_rs", "e_nm", "h2_ok", "hT", "hThi", "hTlo")
        xb_ok, g_ok, gev, tev = sems("xb_ok", "g_ok", "gev", "tev")
        p_st, p_mv, p_ve, p_rs, p_sc, p_nm, p_h = sems("p_st", "p_mv", "p_ve", "p_rs", "p_sc", "p_nm", "p_h")
        lxh_ok, lxl_ok, g2h_ok, g2l_ok, slot_hi, slot_lo, acc1, o_ok = sems(
            "lxh_ok", "lxl_ok", "g2h_ok", "g2l_ok", "slot_hi", "slot_lo", "acc1", "o_ok")

        CH0 = [(k, g) for k in range(NB) for g in range(k // 4 + 1)]
        FIRST0 = [CH0.index((k, 0)) for k in range(NB)] + [len(CH0)]

        def half_of(c):
            return (Xh, Xl) if (c // NB) % 2 == 0 else (Yh, Yl)

        def blocks(ap):
            return ap.rearrange("p (b f) -> p b f", f=F)

        def strip(dram, s, back, q=None):
            a = dram[bass.ds(s.of(1, -back), 1)].rearrange("o p m -> (o p) m")
            return a if q is None else a[:, q * Q:(q + 1) * Q]

        def step_wait(eng, sem, value):
            eng.wait_ge(const0, 1)
            wait(eng, sem, value)

        block = ctx.enter_context(nc.Block())

        @block.sync
        def _(sp):
            x1w = x1[:, 0, :]
            sp.dma_start(x1w[:, 0:F], w_l0).then_inc(ld_w, 16)
            sp.dma_start(x1w[:, F:4 * F].rearrange("p (k o) -> p k o", k=3),
                         w_l1.rearrange("k f o -> f k o")).then_inc(ld_w, 16)
            for k in range(NB):
                if k >= 3:
                    sp.wait_ge(p0S, FIRST0[k - 2])
                sp.dma_start(rowb[:, k % 3, 0:(k + 1) * P], rows_v[k, :, 0:(k + 1) * P]).then_inc(ld_row[k % 3], 16)
                if k:
                    sp.dma_start(colb[:, k % 3, 0:k * P].rearrange("p (j c) -> p j c", c=P),
                                 cols_v[k, :, 0:k, :]).then_inc(ld_col[k % 3], 16)
                sp.dma_start(blocks(hst[:, k, :]), xv[0, k]).then_inc(ld_x0[k], 16)
            sp.dma_start(scal[:, 3, :], bass.AP(adj.tensor, 0, [[N + 1, P], [(N + 1) * P, NB]]),
                         allow_slow_non_contiguous=True).then_inc(ld_diag, 16)
            sp.dma_start(biasb[:, :], bias.partition_broadcast(P)).then_inc(ld_bias, 16)

            def load_next(s, q):
                if s.c < NB:
                    step_wait(sp, rT, s.of(4, q - 3))
                    sp.dma_start(R[:, q, :], rows_v[bass.ds(s.of(1, 0), 1)].rearrange("o p m -> (o p) m")
                                 [:, q * Q:(q + 1) * Q]).then_inc(ld_r[q], 16)
                step_wait(sp, llo, s.of(4, q - 3))
                if 1 <= s.c <= NB:
                    step_wait(sp, st_s[q], s.of(16, 0))
                if s.c < NB:
                    src = cols_v[bass.ds(s.of(1, 0), 1), :, 4 * q:4 * q + 4, :].rearrange("o p j c -> (o p) j c")
                    sp.dma_start(C[:, q, :].rearrange("p (j c) -> p j c", c=P), src).then_inc(ld_c[q], 16)
                elif s.c < L1:
                    if s.c == NB:
                        sp.wait_ge(st_s[q], 16 * NB)
                    sp.dma_start(C[:, q, :], strip(s_dram, s, NB, q)).then_inc(ld_c[q], 16)
                else:
                    if s.c == L1:
                        for p in range(2):
                            sp.wait_ge(st_at[p], 16 * NB // 2)
                    back = L1 if s.c < L1 + NB else L1 + NB
                    sp.dma_start(C[:, q, :], strip(at_dram, s, back, q)).then_inc(ld_c[q], 16)

            for q in range(NQ):
                load_next(Step(None, 0), q)
            sp.dma_start(blocks(xp[:, :]), xv[1, 0]).then_inc(ld_xp, 16)
            for q in range(NQ):
                sp.wait_ge(S_ok, q + 1)
                sp.dma_start(s_dram[0, :, q * Q:(q + 1) * Q], C[:, q, :]).then_inc(st_s[q], 16)
            for q in range(NQ):
                load_next(Step(None, 1), q)

            def body(t):
                c = t.c
                p = c % 2
                if c < NB:
                    step_wait(sp, mk_ok, t.of(1, 1))
                    sp.dma_start(strip(at_dram, t, 0), AT[:, p, :]).then_inc(st_at[p], 16)
                if c > L1:
                    store_out(t)
                for q in range(NQ):
                    if c < NB - 1:
                        step_wait(sp, S_ok, t.of(4, 4 + q + 1))
                        sp.dma_start(strip(s_dram, t, -1, q), C[:, q, :]).then_inc(st_s[q], 16)
                    if q >= 1 and c < LAST - 2:
                        load_next(Step(t.i, c + 2), q - 1)
                    if q == 1 and c < L1:
                        step_wait(sp, x1_ok, t.of(1, 0))
                        if c < NB:
                            src = xv[0, bass.ds(t.of(1, 0), 1)]
                        else:
                            src = xv[1, bass.ds(t.of(1, -NB), 1)]
                        sp.dma_start(blocks(xe[:, :]), src.rearrange("o p b f -> (o p) b f")).then_inc(ld_xe, 16)
                    if q == 1 and c >= L1:
                        if c > L1:
                            step_wait(sp, lxl_ok, t.of(1, 1 - L1))
                        if c < LAST - 1:
                            load_lx(Step(t.i, c + 1))
                        if c == L1:
                            sp.wait_ge(x1_ok, L1)
                            load_g2(t)
                    if q == 2 and 2 <= c < L1 + 2:
                        step_wait(sp, tev, t.of(4, -8 + 4))
                        sp.dma_start(strip(t_dram, t, 2), x1[:, p, :]).then_inc(st_t[p], 16)
                        step_wait(sp, gev, t.of(4, -8 + 4))
                        sp.dma_start(strip(g_dram, t, 2), g12[:, :, :].rearrange("p k w -> p (k w)")).then_inc(st_g, 16)
                    if q == 2 and c < L1 + NB - 1:
                        step_wait(sp, prep_lo, t.of(1, NB + 1))
                        if c < NB - 1:
                            sp.dma_start(blocks(xp[:, :]), xv[1, bass.ds(t.of(1, 1), 1)]
                                         .rearrange("o p b f -> (o p) b f")).then_inc(ld_xp, 16)
                        else:
                            if c >= L1 + 2:
                                sp.wait_ge(st_g, 16 * L1)
                            sp.dma_start(xp[:, :], strip(g_dram, t, NB - 1)[:, 0:W]).then_inc(ld_xp, 16)
                    if q == 3 and c >= L1:
                        if c < L1 + 2:
                            sp.wait_ge(st_t[p], 16 * NB)
                        else:
                            step_wait(sp, st_o[p], t.pair(-L1, 16))
                            if c == L1 + 2:
                                sp.wait_ge(st_t[1], 16 * NB)
                        sp.dma_start(x1[:, p, :], strip(t_dram, t, L1)).then_inc(ld_t[p], 16)
                        if c < LAST - 1:
                            step_wait(sp, g2l_ok, t.of(1, 1 - L1))
                            load_g2(Step(t.i, c + 1))
                if c < LAST - 2:
                    load_next(Step(t.i, c + 2), NQ - 1)
                if c == L1 - 1:
                    load_lx(Step(None, L1))

            def load_lx(s):
                back = L1 if s.c < L1 + NB else L1 + NB
                sp.dma_start(lx[:, :], strip(at_dram, s, back)[:, N:N + P]).then_inc(ld_lx, 16)

            def load_g2(s):
                step_wait(sp, st_g, s.of(16, 16 * (1 - L1)))
                sp.dma_start(xe[:, :], strip(g_dram, s, L1)[:, W:2 * W]).then_inc(ld_g2, 16)

            def store_out(t):
                step_wait(sp, o_ok, t.of(1, -L1))
                if t.c <= L1 + NB:
                    dst = ov[0, bass.ds(t.of(1, -L1 - 1), 1)]
                else:
                    dst = ov[1, bass.ds(t.of(1, -L1 - NB - 1), 1)]
                pp = (t.c - 1) % 2
                sp.dma_start(dst.rearrange("o p b f -> (o p) b f"), blocks(x1[:, pp, :])).then_inc(st_o[pp], 16)

            run_steps(sp, body)
            store_out(Step(None, LAST))
            for p in range(2):
                sp.wait_ge(st_o[p], 16 * NB)
                sp.wait_ge(st_t[p], 16 * NB)
                sp.wait_ge(st_at[p], 16 * NB // 2)
            sp.wait_ge(st_g, 16 * L1)
            for q in range(NQ):
                sp.wait_ge(st_s[q], 16 * NB)

        @block.tensor
        def _(pe):
            mm = nc.tensor.matmul
            pe.wait_ge(ident_ok, 2)
            pe.wait_ge(const0, 4)
            pe.wait_ge(d_zero, 2)

            def row_sums(n):
                k, g = CH0[n]
                pe.wait_ge(p0R, n + 1)
                last = None
                for j in range(4 * g, min(4 * g + 4, k)):
                    last = mm(psD[:, j, k:k + 1], sring[:, n % 4, (j - 4 * g) * P:(j - 4 * g + 1) * P], ones[:, :],
                              start=True, stop=True)
                (last if last is not None else nc.tensor.nop()).then_inc(p0D, 1)

            for n, (k, g) in enumerate(CH0):
                if g == 0:
                    pe.wait_ge(ld_row[k % 3], 16 * (k // 3 + 1))
                    if k:
                        pe.wait_ge(ld_col[k % 3], 16 * (k // 3 + (1 if k % 3 else 0)))
                if n >= 2:
                    pe.wait_ge(p0S, n - 1)
                for j in range(4 * g, min(4 * g + 4, k + 1)):
                    src = rowb[:, k % 3, j * P:(j + 1) * P] if j == k else colb[:, k % 3, j * P:(j + 1) * P]
                    last = nc.tensor.transpose(psA[:, n % 2, (j - 4 * g) * P:(j - 4 * g + 1) * P], src, ident[:, :])
                last.then_inc(p0T, 1)
                if n >= 1:
                    row_sums(n - 1)
            row_sums(len(CH0) - 1)
            pe.wait_ge(p0S, len(CH0))

            def rows_T(s, q):
                wait(pe, ld_r[q], s.of(16, 16))
                wait(pe, at_ok, s.of(4, q - 1))
                for j in range(4):
                    last = nc.tensor.transpose(psA[:, q % 2, j * P:(j + 1) * P], R[:, q, j * P:(j + 1) * P], ident[:, :])
                last.then_inc(rT, 1)

            for q in range(NQ):
                rows_T(Step(None, 0), q)

            def finish(t, q):
                c = t.c
                if q == 0 and 1 <= c <= L1:
                    wait(pe, z_ok, t.of(1, 0))
                    wait(pe, hThi, t.of(1, -1))
                    wait(pe, hTlo, t.of(1, -1))
                    for b in range(HB):
                        last = nc.tensor.transpose(psZ[:, b * F:(b + 1) * F], z[:, b * F:(b + 1) * F], ident[:, :])
                    last.then_inc(zT, 1)
                if q == 1 and 1 <= c <= L1:
                    if c == 1:
                        pe.wait_ge(wlo_ok, 1)
                        pe.wait_ge(d_ok, 1)
                    wait(pe, zThi, t.of(1, 0))
                    wait(pe, zTlo, t.of(1, 0))
                    wait(pe, r1_ok, t.of(1, -1))
                    for b in range(HB):
                        f = slice(b * F, (b + 1) * F)
                        mm(psW[:, f], zTh[:, f], Wh[:, 0:F], start=True, stop=False)
                        mm(psW[:, f], zTh[:, f], Wl[:, 0:F], start=False, stop=False)
                        last = mm(psW[:, f], zTl[:, f], Wh[:, 0:F], start=False, stop=True)
                    last.then_inc(w_ok, 1)
                if q in (0, 2) and 2 <= c < L1 + 2:
                    if q == 0:
                        wait(pe, hThi, t.of(1, -1))
                        wait(pe, hTlo, t.of(1, -1))
                    for b in (q, q + 1):
                        f = slice(b * F, (b + 1) * F)
                        wait(pe, gev, t.of(4, -8 + b - 1))
                        mm(psG[:, b % 2, 0:3 * F], hTh[:, f], Wh[:, F:4 * F], start=True, stop=False)
                        mm(psG[:, b % 2, 0:3 * F], hTh[:, f], Wl[:, F:4 * F], start=False, stop=False)
                        mm(psG[:, b % 2, 0:3 * F], hTl[:, f], Wh[:, F:4 * F], start=False, stop=True).then_inc(g_ok, 1)
                if q == 3 and 1 <= c <= L1:
                    wait(pe, h2_ok, t.of(1, 0))
                    for b in range(HB):
                        last = nc.tensor.transpose(psZ[:, b * F:(b + 1) * F], z[:, b * F:(b + 1) * F], ident[:, :])
                    last.then_inc(hT, 1)

            def body(t):
                c = t.c
                rh, rl = half_of(c)
                acc = psAcc[:, c % 2, :]
                if 2 <= c < L1 + 2:
                    wait(pe, z_ok, t.of(1, -1))
                elif c >= L1 + 2:
                    wait(pe, o_ok, t.of(1, -1 - L1))
                if c > L1 and c != L1 + NB:
                    wait(pe, slot_hi, t.of(1, -L1))
                    wait(pe, slot_lo, t.of(1, -L1))
                for q in range(NQ):
                    wait(pe, lhi, t.of(4, q + 1))
                    wait(pe, llo, t.of(4, q + 1))
                    for j in range(4):
                        k = 4 * q + j
                        lh, ll = Lh[:, q, j * P:(j + 1) * P], Ll[:, q, j * P:(j + 1) * P]
                        if c % NB == 0:
                            pe.wait_ge(prep_hi, c + k + 1)
                            pe.wait_ge(prep_lo, c + k + 1)
                        mm(acc, lh, rh[:, k, :], start=k == 0, stop=False)
                        mm(acc, lh, rl[:, k, :], start=False, stop=False)
                        mm(acc, ll, rh[:, k, :], start=False, stop=c < L1 and k == NB - 1).then_inc(used, 1)
                    if c < NB - 1:
                        rows_T(Step(t.i, c + 1), q)
                    finish(t, q)
                if c >= L1:
                    wait(pe, lxh_ok, t.of(1, 1 - L1))
                    wait(pe, lxl_ok, t.of(1, 1 - L1))
                    wait(pe, g2h_ok, t.of(1, 1 - L1))
                    wait(pe, g2l_ok, t.of(1, 1 - L1))
                    mm(acc, lxh[:, :], zTh[:, :], start=False, stop=False)
                    mm(acc, lxh[:, :], zTl[:, :], start=False, stop=False)
                    mm(acc, lxl[:, :], zTh[:, :], start=False, stop=True).then_inc(acc1, 1)

            run_steps(pe, body)

        @block.scalar
        def _(act):
            A = nc.scalar.activation
            act.wait_ge(ld_w, 32)
            A(Wh[:, :], x1[:, 0, :], ACT.Copy).then_inc(whi_ok, 1)
            act.wait_ge(const0, 4)

            def h0(n):
                act.wait_ge(s0_nm, n + 1)
                for b in range(HB):
                    f = slice(b * F, (b + 1) * F)
                    last = A(hst[:, n, f], hst[:, n, f], ACT.Relu, bias=n0.nm[:, b:b + 1], scale=n0.rs[:, b:b + 1])
                last.then_inc(s0_h, 1)

            for n, (k, g) in enumerate(CH0):
                w = min(4, k + 1 - 4 * g) * P
                act.wait_ge(p0S, n + 1)
                A(sring[:, n % 4, 0:w], sring[:, n % 4, 0:w], ACT.Relu, accum_out=drow[:, k, g:g + 1]).then_inc(p0R, 1)
                if g == k // 4:
                    h0(k)
            act.wait_ge(d_inv, 1)

            def front(s, q):
                if s.c < NB:
                    wait(act, rT, s.of(4, q + 1))
                    if q == 0:
                        wait(act, st_at[s.c % 2], s.pair(0, 16))
                    A(AT[:, s.c % 2, q * Q:(q + 1) * Q], psA[:, q % 2, :], ACT.Copy).then_inc(at_ok, 1)
                    wait(act, S_ok, s.of(4, q + 1))
                else:
                    wait(act, ld_c[q], s.of(16, 16))
                wait(act, used, s.of(16, -16 + 4 * q + 4) if s.c else 0)
                A(Lh[:, q, :], C[:, q, :], ACT.Relu if s.c < L1 else ACT.Copy).then_inc(lhi, 1)

            for q in range(NQ):
                front(Step(None, 0), q)
            for n in range(NB):
                act.wait_ge(s0_h, n + 1)
                A(Xh[:, n, :], hst[:, n, :], ACT.Relu, scale=scal[:, 0, n:n + 1]).then_inc(prep_hi, 1)

            def body(t):
                c = t.c
                p = c % 2
                pe_ = (c - 1) % 2
                if c >= L1:
                    wait(act, ld_lx, t.of(16, 16 * (1 - L1)))
                    wait(act, acc1, t.of(1, -L1))
                    A(lxh[:, :], lx[:, :], ACT.Copy).then_inc(lxh_ok, 1)
                for q in range(NQ):
                    if q == 3 and c >= L1:
                        slot(t)
                    if c < LAST - 1:
                        front(Step(t.i, c + 1), q)
                    if q == 0 and 1 <= c <= L1:
                        wait(act, zT, t.of(1, 0))
                        wait(act, w_ok, t.of(1, -1))
                        A(zTh[:, :], psZ[:, :], ACT.Copy).then_inc(zThi, 1)
                    if q in (0, 2) and 2 <= c < L1 + 2:
                        for b in (q, q + 1):
                            wait(act, tev, t.of(4, -8 + b + 1))
                            if b == 0:
                                wait(act, st_g, t.of(16, -32))
                            A(g12[:, :, b * F:(b + 1) * F],
                              psG[:, b % 2, F:3 * F].rearrange("p (k f) -> p k f", k=2), ACT.Copy).then_inc(gev, 1)
                    if q == 1 and 1 <= c <= L1:
                        wait(act, w_ok, t.of(1, 0))
                        wait(act, cur_ok, t.of(1, 0))
                        if c >= 3:
                            wait(act, st_t[pe_], t.pair(-1, 16))
                        elif c == 1:
                            act.wait_ge(wlo_ok, 1)
                        A(x1[:, pe_, :], psW[:, :], ACT.Relu, scale=cur_e[:, 2:3]).then_inc(r1_ok, 1)
                    if q == 2 and 1 <= c <= L1:
                        wait(act, e_nm, t.of(1, 0))
                        wait(act, zT, t.of(1, 0))
                        for b in range(HB):
                            f = slice(b * F, (b + 1) * F)
                            last = A(z[:, f], x1[:, pe_, f], ACT.Relu, bias=ne.nm[:, b:b + 1], scale=ne.rs[:, b:b + 1])
                        last.then_inc(h2_ok, 1)
                    if q == 1 and c < L1 + NB:
                        prep(t)
                    if q == 2 and c >= L1:
                        wait(act, ld_g2, t.of(16, 16 * (1 - L1)))
                        if c == L1:
                            act.wait_ge(w_ok, L1)
                        else:
                            wait(act, acc1, t.of(1, -L1))
                            wait(act, slot_hi, t.of(1, -L1))
                        A(zTh[:, :], xe[:, :], ACT.Copy).then_inc(g2h_ok, 1)
                    if q == 3 and 1 <= c <= L1:
                        wait(act, hT, t.of(1, 0))
                        wait(act, g_ok, t.of(4, -4))
                        A(hTh[:, :], psZ[:, :], ACT.Copy).then_inc(hThi, 1)

            def prep(t):
                c = t.c
                dst, _ = half_of(c + NB)
                if c < NB:
                    wait(act, p_nm, t.of(1, 1))
                    for b in range(HB):
                        f = slice(b * F, (b + 1) * F)
                        last = A(xp[:, f], xp[:, f], ACT.Relu, bias=npn.nm[:, b:b + 1], scale=npn.rs[:, b:b + 1])
                    last.then_inc(p_h, 1)
                    wait(act, p_h, t.of(1, 1))
                    off = t.of(1, 0)
                else:
                    wait(act, ld_xp, t.of(16, 16))
                    act.wait_ge(used, NB * (c // NB) * NB)
                    if c < L1:
                        wait(act, hsum, t.of(1, 1 - NB))
                    else:
                        wait(act, hsum, t.of(1, 1 - NB))
                    off = t.of(1, -(c // NB) * NB)
                A(dst[:, bass.ds(off, 1), :], xp[:, :].rearrange("p (o w) -> p o w", o=1), ACT.Copy).then_inc(prep_hi, 1)

            def slot(t):
                dst, _ = half_of(t.c)
                back = L1 if t.c < L1 + NB else L1 + NB
                wait(act, used, t.of(17, 1 - back))
                wait(act, g2h_ok, t.of(1, 1 - L1))
                A(dst[:, bass.ds(t.of(1, -back), 1), :], zTh[:, :].bitcast(F32).rearrange("p (o w) -> p o w", o=1),
                  ACT.Copy).then_inc(slot_hi, 1)

            run_steps(act, body)

        @block.vector
        def _(dve):
            V = nc.vector

            def stats(nrm, src, st, mv, ve, seen):
                for b in range(HB):
                    last = V.bn_stats(nrm.st[:, b, :], src[:, b * F:(b + 1) * F])
                last.then_inc(st, 1)
                step_wait(dve, st, seen)
                for b in range(HB):
                    last = V.bn_aggr(nrm.mv[:, b, :], nrm.st[:, b, :])
                last.then_inc(mv, 1)
                wait(dve, mv, seen)
                V.tensor_scalar(nrm.ve[:, :], nrm.mv[:, :, 1], EPS, None, ALU.add).then_inc(ve, 1)

            def neg_mean(nrm, sem):
                V.scalar_tensor_tensor(out=nrm.nm[:, :], in0=nrm.mv[:, :, 0], scalar=-1.0, in1=nrm.rs[:, :],
                                       op0=ALU.mult, op1=ALU.mult).then_inc(sem, 1)

            V.memset(psD[:, :, :], 0.0).then_inc(d_zero, 1)
            V.memset(drow[:, :, :], 0.0).then_inc(d_zero, 1)
            V.memset(ones[:, :], 1.0).then_inc(const0, 1)
            dve.wait_ge(whi_ok, 1)
            V.tensor_tensor(Wl[:, :], x1[:, 0, :], Wh[:, :].bitcast(F32), ALU.subtract).then_inc(wlo_ok, 1)
            dve.wait_ge(d_zero, 2)
            for n, (k, g) in enumerate(CH0):
                w = min(4, k + 1 - 4 * g) * P
                dve.wait_ge(p0T, n + 1)
                if n >= 4:
                    dve.wait_ge(p0D, n - 3)
                V.tensor_tensor(sring[:, n % 4, 0:w], psA[:, n % 2, 0:w], rowb[:, k % 3, 4 * g * P:4 * g * P + w],
                                ALU.add).then_inc(p0S, 1)
                if g == k // 4:
                    dve.wait_ge(ld_x0[k], 16)
                    if k:
                        dve.wait_ge(s0_h, k)
                    stats(n0, hst[:, k, :], s0_st, s0_mv, s0_ve, k + 1)
                    dve.wait_ge(s0_rs, k + 1)
                    neg_mean(n0, s0_nm)
            dve.wait_ge(p0D, len(CH0))
            V.reduce_sum(d1[:, :], psD[:, :, :], axis=AX.X).then_inc(d_sums, 1)
            dve.wait_ge(p0R, len(CH0))
            V.reduce_sum(d2[:, :], drow[:, :, :], axis=AX.X).then_inc(d_sums, 1)
            dve.wait_ge(d_sums, 2)
            V.tensor_tensor(d1[:, :], d1[:, :], d2[:, :], ALU.add).then_inc(d_sum, 1)
            dve.wait_ge(d_sum, 1)
            V.tensor_scalar(d2[:, :], d1[:, :], 0.0, None, ALU.is_le).then_inc(d_none, 1)
            dve.wait_ge(d_none, 1)
            V.scalar_tensor_tensor(out=dsafe[:, :], in0=d1[:, :], scalar=0.5, in1=d2[:, :],
                                   op0=ALU.mult, op1=ALU.add).then_inc(d_safe, 1)
            dve.wait_ge(d_inv, 1)
            V.scalar_tensor_tensor(out=scal[:, 1, :], in0=scal[:, 0, :], scalar=-0.5, in1=scal[:, 0, :],
                                   op0=ALU.mult, op1=ALU.mult).then_inc(d_ok, 1)

            def front(s, q):
                if s.c < NB:
                    wait(dve, at_ok, s.of(4, q + 1))
                    wait(dve, ld_c[q], s.of(16, 16))
                    V.tensor_tensor(C[:, q, :], AT[:, s.c % 2, q * Q:(q + 1) * Q], C[:, q, :],
                                    ALU.add).then_inc(S_ok, 1)
                wait(dve, lhi, s.of(4, q + 1))
                if s.c < L1:
                    V.scalar_tensor_tensor(out=Ll[:, q, :], in0=C[:, q, :], scalar=0.0, in1=Lh[:, q, :].bitcast(F32),
                                           op0=ALU.max, op1=ALU.subtract).then_inc(llo, 1)
                else:
                    V.tensor_tensor(Ll[:, q, :], C[:, q, :], Lh[:, q, :].bitcast(F32), ALU.subtract).then_inc(llo, 1)

            for q in range(NQ):
                front(Step(None, 0), q)
            for n in range(NB):
                dve.wait_ge(prep_hi, n + 1)
                V.scalar_tensor_tensor(out=Xl[:, n, :], in0=hst[:, n, :], scalar=scal[:, 0, n:n + 1],
                                       in1=Xh[:, n, :].bitcast(F32), op0=ALU.mult, op1=ALU.subtract).then_inc(prep_lo, 1)
            dve.wait_ge(ld_diag, 16)
            dve.wait_ge(d_sq, 1)
            dve.wait_ge(d_ok, 1)

            def pick(dst, t, shift):
                back = shift + NB * ((t.c - shift) // NB)
                o = t.of(1, -back)
                return V.tensor_copy(dst[:, :].rearrange("p (k o) -> p k o", o=1), scal[:, :, bass.ds(o, 1)])

            def t_out(t, b):
                f = slice(b * F, (b + 1) * F)
                wait(dve, g_ok, t.of(4, -8 + b + 1))
                V.scalar_tensor_tensor(out=x1[:, t.c % 2, f], in0=psG[:, b % 2, 0:F], scalar=cur_g[:, 3:4],
                                       in1=x1[:, t.c % 2, f], op0=ALU.mult, op1=ALU.add).then_inc(tev, 1)

            def body(t):
                c = t.c
                p, pe_ = c % 2, (c - 1) % 2
                if c < L1 + 2:
                    if c >= 2:
                        pick(cur_g, t, 2)
                    if c < NB:
                        pick(cur_p, t, 0)
                    if 1 <= c <= L1:
                        pick(cur_e, t, 1)
                    V.tensor_copy(d2[:, 0:1], ones[:, :]).then_inc(cur0, 1)
                    wait(dve, cur0, t.of(1, 1))
                if 1 <= c <= L1:
                    V.tensor_copy(d2[:, 1:2], ones[:, :]).then_inc(cur_ok, 1)
                    hi, lo = half_of(c - 1)
                    o = t.of(1, -1 - NB * ((c - 1) // NB))
                    wait(dve, hT, t.of(1, -1))
                    V.tensor_tensor(z[:, :].rearrange("p (o w) -> p o w", o=1), hi[:, bass.ds(o, 1), :].bitcast(F32),
                                    lo[:, bass.ds(o, 1), :].bitcast(F32), ALU.add).then_inc(hsum, 1)
                    wait(dve, hsum, t.of(1, 0))
                    wait(dve, used, t.of(16, 0))
                    V.scalar_tensor_tensor(out=z[:, :], in0=psAcc[:, pe_, :], scalar=cur_e[:, 1:2], in1=z[:, :],
                                           op0=ALU.mult, op1=ALU.add).then_inc(z_ok, 1)
                if c > L1:
                    result(t)
                if c >= L1:
                    wait(dve, lxh_ok, t.of(1, 1 - L1))
                    V.tensor_tensor(lxl[:, :], lx[:, :], lxh[:, :].bitcast(F32), ALU.subtract).then_inc(lxl_ok, 1)
                for q in range(NQ):
                    if q == 0 and c < NB:
                        wait(dve, ld_xp, t.of(16, 16))
                        stats(npn, xp, p_st, p_mv, p_ve, t.of(1, 1))
                    if q == 3 and c >= L1:
                        slot(t)
                    if c < LAST - 1:
                        front(Step(t.i, c + 1), q)
                    if q == 0 and 1 <= c <= L1:
                        wait(dve, zThi, t.of(1, 0))
                        V.tensor_tensor(zTl[:, :], psZ[:, :], zTh[:, :].bitcast(F32), ALU.subtract).then_inc(zTlo, 1)
                    if q in (0, 2) and 2 <= c < L1 + 2:
                        if q == 0:
                            wait(dve, xb_ok, t.of(1, -1))
                        t_out(t, q)
                        t_out(t, q + 1)
                    if q == 0 and c < NB:
                        wait(dve, p_rs, t.of(1, 1))
                        V.tensor_scalar(npn.rs[:, :], npn.rs[:, :], cur_p[:, 0:1], None, ALU.mult).then_inc(p_sc, 1)
                        wait(dve, p_sc, t.of(1, 1))
                        neg_mean(npn, p_nm)
                    if q == 1 and 1 <= c <= L1:
                        wait(dve, r1_ok, t.of(1, 0))
                        wait(dve, ld_xe, t.of(16, 0))
                        V.tensor_tensor(x1[:, pe_, :], x1[:, pe_, :], xe[:, :], ALU.add).then_inc(x1_ok, 1)
                        wait(dve, x1_ok, t.of(1, 0))
                        stats(ne, x1[:, pe_, :], e_st, e_mv, e_ve, t.of(1, 0))
                        wait(dve, e_rs, t.of(1, 0))
                        neg_mean(ne, e_nm)
                    if q == 2 and c < L1 + NB:
                        _, dst = half_of(c + NB)
                        wait(dve, prep_hi, t.of(1, NB + 1))
                        o = t.of(1, -(c // NB) * NB)
                        hi, _ = half_of(c + NB)
                        V.tensor_tensor(dst[:, bass.ds(o, 1), :], xp[:, :].rearrange("p (o w) -> p o w", o=1),
                                        hi[:, bass.ds(o, 1), :].bitcast(F32), ALU.subtract).then_inc(prep_lo, 1)
                    if q == 2 and c >= L1:
                        wait(dve, g2h_ok, t.of(1, 1 - L1))
                        wait(dve, slot_lo, t.of(1, -L1))
                        V.tensor_tensor(zTl[:, :], xe[:, :], zTh[:, :].bitcast(F32), ALU.subtract).then_inc(g2l_ok, 1)
                    if q == 3 and 1 <= c <= L1:
                        wait(dve, hThi, t.of(1, 0))
                        V.tensor_tensor(hTl[:, :], psZ[:, :], hTh[:, :].bitcast(F32), ALU.subtract).then_inc(hTlo, 1)

            def slot(t):
                _, dst = half_of(t.c)
                back = L1 if t.c < L1 + NB else L1 + NB
                wait(dve, used, t.of(17, 1 - back))
                wait(dve, g2l_ok, t.of(1, 1 - L1))
                V.tensor_copy(dst[:, bass.ds(t.of(1, -back), 1), :],
                              zTl[:, :].bitcast(F32).rearrange("p (o w) -> p o w", o=1)).then_inc(slot_lo, 1)

            def result(t):
                pp = (t.c - 1) % 2
                wait(dve, acc1, t.of(1, -L1))
                wait(dve, ld_t[pp], t.pair(-1 - L1, 16) + 16)
                V.tensor_tensor(x1[:, pp, :], psAcc[:, pp, :], x1[:, pp, :], ALU.add).then_inc(o_ok, 1)

            run_steps(dve, body)
            result(Step(None, LAST))

        @block.gpsimd
        def _(pool):
            G = nc.gpsimd
            G.memset(mhalf[:, :], -0.5).then_inc(const0, 1)
            G.memset(half[:, :], 0.5).then_inc(const0, 1)
            G.memset(ident[:, :], 0.0).then_inc(ident_ok, 1)
            pool.wait_ge(ident_ok, 1)
            G.affine_select(out=ident[:, :], in_=ident[:, :], compare_op=ALU.not_equal, fill=1.0,
                            base=0, pattern=[[-1, P]], channel_multiplier=1).then_inc(ident_ok, 1)
            G.memset(dup[:, :], 0.0).then_inc(const0, 1)
            pool.wait_ge(const0, 4)

            def power(out, base, exponent):
                return G.tensor_tensor(out=out, in0=base, in1=exponent, op=ALU.pow)

            for n in range(NB):
                pool.wait_ge(s0_ve, n + 1)
                power(n0.rs[:, :], n0.ve[:, :], mhalf[:, 0:HB]).then_inc(s0_rs, 1)
            pool.wait_ge(d_safe, 1)
            power(scal[:, 0, :], dsafe[:, :], mhalf[:, :]).then_inc(d_inv, 1)
            power(scal[:, 2, :], dsafe[:, :], half[:, :]).then_inc(d_sq, 1)

            def masks(s):
                p = s.c % 2
                wait(pool, S_ok, s.of(4, 4))
                at = AT[:, p, :].rearrange("p (j c) -> p j c", c=P)
                if not isinstance(s.of(1, 0), int) or s.c:
                    step_wait(pool, mk_ok, s.of(1, 0))
                G.tensor_copy(dmid[:, :].rearrange("p (o c) -> p o c", o=1), at[:, bass.ds(s.of(1, 0), 1), :]).then_inc(mk_c, 1)
                wait(pool, mk_c, s.of(1, 1))
                G.tensor_tensor(out=tiny[:, :], in0=half[:, 0:1], in1=half[:, 0:1], op=ALU.add)
                G.affine_select(out=dup[:, :], in_=dmid[:, :], compare_op=ALU.is_gt, fill=0.0,
                                base=0, pattern=[[-1, P]], channel_multiplier=1)
                G.affine_select(out=AT[:, p, N:N + P], in_=dmid[:, :], compare_op=ALU.is_gt, fill=0.0,
                                base=0, pattern=[[1, P]], channel_multiplier=-1).then_inc(mk_s, 1)
                step_wait(pool, mk_s, s.of(1, 1))
                G.tensor_copy(at[:, bass.ds(s.of(1, 0), 1), :], dup[:, :].rearrange("p (o c) -> p o c", o=1)).then_inc(mk_ok, 1)

            masks(Step(None, 0))
            pool.wait_ge(ld_bias, 16)

            def body(t):
                c = t.c
                pe_ = (c - 1) % 2
                if c < NB:
                    wait(pool, p_ve, t.of(1, 1))
                    power(npn.rs[:, :], npn.ve[:, :], mhalf[:, 0:HB]).then_inc(p_rs, 1)
                if 1 <= c <= L1:
                    wait(pool, e_ve, t.of(1, 0))
                    power(ne.rs[:, :], ne.ve[:, :], mhalf[:, 0:HB]).then_inc(e_rs, 1)
                    wait(pool, h2_ok, t.of(1, 0))
                    G.tensor_tensor(out=blocks(x1[:, pe_, :]), in0=blocks(x1[:, pe_, :]),
                                    in1=biasb[:, :].unsqueeze(1).to_broadcast([P, HB, F]), op=ALU.add).then_inc(xb_ok, 1)
                if c < NB - 1:
                    masks(Step(t.i, c + 1))

            for c in (0, 1, 2, 3):
                body(Step(None, c))
            with pool.Fori(0, 5) as i:
                for c in (4, 5):
                    body(Step(i, c))
            for c in (14, 15, 16, 17):
                body(Step(None, c))
            with pool.Fori(0, 6) as i:
                for c in (18, 19):
                    body(Step(i, c))
            for c in (30, 31, 32):
                body(Step(None, c))


_INS = ["x", "adj", "L0_gnn_W", "L1_gnn_W", "L1_gnn_bias"]


def kernel(**inputs):
    import numpy as _np
    import concourse.bacc as _bacc
    from concourse import mybir as _mybir
    from concourse.bass_utils import run_bass_kernel_spmd as _run

    nc = _bacc.Bacc("TRN2", target_bir_lowering=False, num_devices=1)
    arrays, args = {}, []
    for name in _INS:
        a = _np.ascontiguousarray(inputs[name])
        arrays[f"in_{name}"] = a
        args.append(nc.dram_tensor(f"in_{name}", a.shape, _mybir.dt.from_np(a.dtype), kind="ExternalInput").ap())
    args.append(nc.dram_tensor("result", (B, N, F), _mybir.dt.float32, kind="ExternalOutput").ap())
    build(nc, *args)
    r = _run(nc, [arrays], core_ids=[0])
    return r.results[0]["result"]
```

```python
import numpy as np
from contextlib import ExitStack

import concourse.bass as bass
from concourse import mybir

F32 = mybir.dt.float32
F32R = mybir.dt.float32r
ALU = mybir.AluOpType
ACT = mybir.ActivationFunctionType
AX = mybir.AxisListType

P = 128
B, N, F = 8, 2048, 128
NB = N // P
HB = B // 2
W = HB * F
NQ = 4
Q = N // NQ
EPS = 1e-5
L1 = 2 * NB
LAST = 4 * NB


class Step:

    def __init__(self, i, c):
        self.i, self.c = i, c

    def of(self, mul, add):
        return mul * self.c + add if self.i is None else self.i * (2 * mul) + (mul * self.c + add)

    def pair(self, shift, mul):
        k = mul * ((self.c + shift) // 2)
        return k if self.i is None else self.i * mul + k


def wait(eng, sem, value):
    if isinstance(value, int) and value <= 0:
        return
    eng.wait_ge(sem, value)


def run_steps(eng, body):
    def loop(first, last):
        with eng.Fori(0, (last - first) // 2) as i:
            for c in (first, first + 1):
                body(Step(i, c))

    def single(*steps):
        for c in steps:
            body(Step(None, c))

    single(0, 1, 2, 3)
    loop(4, 14)
    single(14, 15, 16, 17)
    loop(18, 30)
    single(30, 31, 32, 33)
    loop(34, 46)
    single(46, 47, 48, 49)
    loop(50, 62)
    single(62, 63)


def build(nc, x, adj, w_l0, w_l1, bias, out):
    s_dram = nc.dram_tensor("s_dram", (NB, P, N), F32, kind="Internal").ap()
    at_dram = nc.dram_tensor("at_dram", (NB, P, N + P), F32, kind="Internal").ap()
    t_dram = nc.dram_tensor("t_dram", (L1, P, W), F32, kind="Internal").ap()
    g_dram = nc.dram_tensor("g_dram", (L1, P, 2 * W), F32, kind="Internal").ap()

    xv = x.rearrange("(h b) (n p) f -> h n p b f", b=HB, p=P)
    ov = out.rearrange("(h b) (n p) f -> h n p b f", b=HB, p=P)
    rows_v = adj.rearrange("(n p) m -> n p m", p=P)
    cols_v = adj.rearrange("(j p) (n c) -> n p j c", p=P, c=P)

    ctx = ExitStack()
    with ctx:
        def sb(name, shape, dt=F32, at=ctx):
            return at.enter_context(nc.sbuf_tensor(name, shape, dt))

        def sems(*names):
            return [ctx.enter_context(nc.semaphore(n)) for n in names]

        def many(name, n):
            return [ctx.enter_context(nc.semaphore(f"{name}{k}")) for k in range(n)]

        class Norm:
            def __init__(self, n, at=ctx):
                self.st, self.mv = sb(n + "_st", [P, HB, 6], at=at), sb(n + "_mv", [P, HB, 2], at=at)
                self.ve, self.rs, self.nm = (sb(n + k, [P, HB], at=at) for k in ("_ve", "_rs", "_nm"))

        Xh = sb("Xh", [P, NB, W], F32R)
        with ExitStack() as early:
            hst = sb("hst", [P, NB, W], at=early)
            rowb = sb("rowb", [P, 3, N], at=early)
            colb = sb("colb", [P, 3, N], at=early)
            sring = sb("sring", [P, 4, 4 * P], at=early)
            drow = sb("drow", [P, NB, NQ], at=early)
            n0s = [Norm("n0", early), Norm("n1", early)]
        Xl = sb("Xl", [P, NB, W], F32R)
        Yh = sb("Yh", [P, NB, W], F32R)
        Yl = sb("Yl", [P, NB, W], F32R)
        Lh = sb("Lh", [P, NQ, Q], F32R)
        Ll = sb("Ll", [P, NQ, Q], F32R)
        C = sb("C", [P, NQ, Q])
        with ExitStack() as layer0:
            R = sb("R", [P, NQ, Q], at=layer0)
        lx = sb("lx", [P, P])
        lxh, lxl = sb("lxh", [P, P], F32R), sb("lxl", [P, P], F32R)
        g2 = sb("g2", [P, W])
        g2h, g2l = sb("g2h", [P, W], F32R), sb("g2l", [P, W], F32R)
        sb("pad", [P, NQ * Q - 3 * P - 3 * W])
        AT = sb("AT", [P, 2, N + P])
        zTh, zTl = sb("zTh", [P, W], F32R), sb("zTl", [P, W], F32R)
        hTh, hTl = sb("hTh", [P, W], F32R), sb("hTl", [P, W], F32R)
        z = sb("z", [P, W])
        h2 = sb("h2", [P, W])
        x1 = sb("x1", [P, 2, W])
        xe = sb("xe", [P, W])
        xp = sb("xp", [P, W])
        g12 = sb("g12", [P, 2, W])
        Wh, Wl = sb("Wh", [P, 4 * F], F32R), sb("Wl", [P, 4 * F], F32R)
        biasb = sb("biasb", [P, F])
        ident = sb("ident", [P, P])
        dmid = sb("dmid", [P, P])
        scal = sb("scal", [P, 4, NB])
        cur_e, cur_g, cur_p = sb("cur_e", [P, 4]), sb("cur_g", [P, 4]), sb("cur_p", [P, 4])
        ones = sb("ones", [P, 1])
        tiny = sb("tiny", [P, 1])
        mhalf, half = sb("mhalf", [P, NB]), sb("half", [P, NB])
        d1, d2 = sb("d1", [P, NB]), sb("d2", [P, NB])
        dsafe = sb("dsafe", [P, NB])

        ne, npn = Norm("ne"), Norm("np")

        psAcc = ctx.enter_context(nc.psum_tensor("psAcc", [P, 2, W], F32))
        psA = ctx.enter_context(nc.psum_tensor("psA", [P, 2, 4 * P], F32))
        psZ = ctx.enter_context(nc.psum_tensor("psZ", [P, W], F32))
        psW = ctx.enter_context(nc.psum_tensor("psW", [P, W], F32))
        psG = ctx.enter_context(nc.psum_tensor("psG", [P, 2, 512], F32))
        psD = psW[:, 0:NB * NB].rearrange("p (j k) -> p j k", k=NB)

        ld_row, ld_col = many("ld_row", 3), many("ld_col", 3)
        ld_x0 = many("ld_x0_", NB)
        ld_c, ld_r, st_s = many("ld_c", NQ), many("ld_r", NQ), many("st_s", NQ)
        st_at, st_t, ld_t, st_o = many("st_at", 2), many("st_t", 2), many("ld_t", 2), many("st_o", 2)
        ld_w, ld_diag, ld_bias, ld_xe, ld_xp, st_g, ld_g2, ld_lx = sems(
            "ld_w", "ld_diag", "ld_bias", "ld_xe", "ld_xp", "st_g", "ld_g2", "ld_lx")
        const0, ident_ok, whi_ok, wlo_ok, d_zero = sems("const0", "ident_ok", "whi_ok", "wlo_ok", "d_zero")
        p0T, p0S, p0R, p0D = sems("p0T", "p0S", "p0R", "p0D")
        s0_st, s0_mv, s0_ve, s0_rs, s0_nm, s0_h = sems("s0_st", "s0_mv", "s0_ve", "s0_rs", "s0_nm", "s0_h")
        d_sums, d_sum, d_none, d_safe, d_inv, d_sq, d_ok = sems(
            "d_sums", "d_sum", "d_none", "d_safe", "d_inv", "d_sq", "d_ok")
        rT, S_ok, at_ok, lhi, llo, used = sems("rT", "S_ok", "at_ok", "lhi", "llo", "used")
        mk_c, mk_s, mk_ok = sems("mk_c", "mk_s", "mk_ok")
        prep_hi, prep_lo = sems("prep_hi", "prep_lo")
        cur_ok, hsum, z_ok, zT, zThi, zTlo, w_ok, r1_ok, x1_ok = sems(
            "cur_ok", "hsum", "z_ok", "zT", "zThi", "zTlo", "w_ok", "r1_ok", "x1_ok")
        e_st, e_mv, e_ve, e_rs, e_nm, h2_ok, hT, hThi, hTlo = sems(
            "e_st", "e_mv", "e_ve", "e_rs", "e_nm", "h2_ok", "hT", "hThi", "hTlo")
        xb_ok, g_ok, gev, tev = sems("xb_ok", "g_ok", "gev", "tev")
        p_st, p_mv, p_ve, p_rs, p_sc, p_nm, p_h = sems("p_st", "p_mv", "p_ve", "p_rs", "p_sc", "p_nm", "p_h")
        lxh_ok, lxl_ok, g2h_ok, g2l_ok, slot_hi, slot_lo, acc1, o_ok = sems(
            "lxh_ok", "lxl_ok", "g2h_ok", "g2l_ok", "slot_hi", "slot_lo", "acc1", "o_ok")

        CH0 = [(k, g) for k in range(NB) for g in range(k // 4 + 1)]
        FIRST0 = [CH0.index((k, 0)) for k in range(NB)] + [len(CH0)]

        def half_of(c):
            return (Xh, Xl) if (c // NB) % 2 == 0 else (Yh, Yl)

        def blocks(ap):
            return ap.rearrange("p (b f) -> p b f", f=F)

        def strip(dram, s, back, q=None):
            a = dram[bass.ds(s.of(1, -back), 1)].rearrange("o p m -> (o p) m")
            return a if q is None else a[:, q * Q:(q + 1) * Q]

        def step_wait(eng, sem, value):
            eng.wait_ge(const0, 1)
            wait(eng, sem, value)

        block = ctx.enter_context(nc.Block())

        @block.sync
        def _(sp):
            x1w = x1[:, 0, :]
            sp.dma_start(x1w[:, 0:F], w_l0).then_inc(ld_w, 16)
            sp.dma_start(x1w[:, F:4 * F].rearrange("p (k o) -> p k o", k=3),
                         w_l1.rearrange("k f o -> f k o")).then_inc(ld_w, 16)
            def load0(k):
                if k >= 3:
                    sp.wait_ge(p0S, FIRST0[k - 2])
                sp.dma_start(rowb[:, k % 3, 0:(k + 1) * P], rows_v[k, :, 0:(k + 1) * P]).then_inc(ld_row[k % 3], 16)
                if k:
                    sp.dma_start(colb[:, k % 3, 0:k * P].rearrange("p (j c) -> p j c", c=P),
                                 cols_v[k, :, 0:k, :]).then_inc(ld_col[k % 3], 16)
                sp.dma_start(blocks(hst[:, k, :]), xv[0, k]).then_inc(ld_x0[k], 16)

            def load_next(s, q):
                if s.c < NB:
                    step_wait(sp, rT, s.of(4, q - 3))
                    sp.dma_start(R[:, q, :], rows_v[bass.ds(s.of(1, 0), 1)].rearrange("o p m -> (o p) m")
                                 [:, q * Q:(q + 1) * Q]).then_inc(ld_r[q], 16)
                step_wait(sp, llo, s.of(4, q - 3))
                if 1 <= s.c <= NB:
                    step_wait(sp, st_s[q], s.of(16, 0))
                if s.c < NB:
                    src = cols_v[bass.ds(s.of(1, 0), 1), :, 4 * q:4 * q + 4, :].rearrange("o p j c -> (o p) j c")
                    sp.dma_start(C[:, q, :].rearrange("p (j c) -> p j c", c=P), src).then_inc(ld_c[q], 16)
                elif s.c < L1:
                    if s.c == NB:
                        sp.wait_ge(st_s[q], 16 * NB)
                    sp.dma_start(C[:, q, :], strip(s_dram, s, NB, q)).then_inc(ld_c[q], 16)
                else:
                    if s.c == L1:
                        for p in range(2):
                            sp.wait_ge(st_at[p], 16 * NB // 2)
                    back = L1 if s.c < L1 + NB else L1 + NB
                    sp.dma_start(C[:, q, :], strip(at_dram, s, back, q)).then_inc(ld_c[q], 16)

            for k in range(NB - 1):
                load0(k)
            for q in range(NQ):
                load_next(Step(None, 0), q)
            load0(NB - 1)
            sp.dma_start(scal[:, 3, :], bass.AP(adj.tensor, 0, [[N + 1, P], [(N + 1) * P, NB]]),
                         allow_slow_non_contiguous=True).then_inc(ld_diag, 16)
            sp.dma_start(biasb[:, :], bias.partition_broadcast(P)).then_inc(ld_bias, 16)
            sp.dma_start(blocks(xp[:, :]), xv[1, 0]).then_inc(ld_xp, 16)
            for q in range(NQ):
                sp.wait_ge(S_ok, q + 1)
                sp.dma_start(s_dram[0, :, q * Q:(q + 1) * Q], C[:, q, :]).then_inc(st_s[q], 16)
            for q in range(NQ - 1):
                load_next(Step(None, 1), q)

            def store_s(s, q):
                step_wait(sp, S_ok, s.of(4, q + 1))
                sp.dma_start(strip(s_dram, s, 0, q), C[:, q, :]).then_inc(st_s[q], 16)

            def body(t):
                c = t.c
                p = c % 2
                nxt = Step(t.i, c + 1)
                if 1 <= c < NB:
                    store_s(t, NQ - 1)
                if c > L1:
                    store_out(t)
                if c < NB - 1:
                    store_s(nxt, 0)
                if c < LAST - 1:
                    load_next(nxt, NQ - 1)
                if c < NB:
                    step_wait(sp, mk_ok, t.of(1, 1))
                    sp.dma_start(strip(at_dram, t, 0), AT[:, p, :]).then_inc(st_at[p], 16)
                for q in range(1, NQ):
                    if c < NB - 1 and q < NQ - 1:
                        store_s(nxt, q)
                    if c < LAST - 2:
                        load_next(Step(t.i, c + 2), q - 1)
                    if q == 1 and c >= L1 + 2:
                        load_t(t)
                    if q == 2 and c < L1:
                        step_wait(sp, x1_ok, t.of(1, 0))
                        if c < NB:
                            src = xv[0, bass.ds(t.of(1, 0), 1)]
                        else:
                            src = xv[1, bass.ds(t.of(1, -NB), 1)]
                        sp.dma_start(blocks(xe[:, :]), src.rearrange("o p b f -> (o p) b f")).then_inc(ld_xe, 16)
                    if q == 2 and c < NB - 1:
                        step_wait(sp, prep_lo, t.of(1, NB + 1))
                        sp.dma_start(blocks(xp[:, :]), xv[1, bass.ds(t.of(1, 1), 1)]
                                     .rearrange("o p b f -> (o p) b f")).then_inc(ld_xp, 16)
                    if q == 2 and L1 <= c < LAST - 1:
                        step_wait(sp, lxl_ok, t.of(1, 1 - L1))
                        load_lx(nxt)
                        step_wait(sp, g2l_ok, t.of(1, 1 - L1))
                        load_g2(nxt)
                    if q == 3 and 2 <= c < L1 + 2:
                        step_wait(sp, tev, t.of(4, -8 + 4))
                        sp.dma_start(strip(t_dram, t, 2), x1[:, p, :]).then_inc(st_t[p], 16)
                        step_wait(sp, gev, t.of(4, -8 + 4))
                        sp.dma_start(strip(g_dram, t, 2), g12[:, :, :].rearrange("p k w -> p (k w)")).then_inc(st_g, 16)
                    if q == 3 and NB - 1 <= c < L1 + NB - 1:
                        step_wait(sp, prep_lo, t.of(1, NB + 1))
                        if c >= L1 + 2:
                            sp.wait_ge(st_g, 16 * L1)
                        sp.dma_start(xp[:, :], strip(g_dram, t, NB - 1)[:, 0:W]).then_inc(ld_xp, 16)
                if L1 <= c < L1 + 2:
                    load_t(t)
                if c == L1 - 1:
                    load_lx(nxt)
                    load_g2(nxt)

            def load_t(t):
                p = t.c % 2
                sp.wait_ge(st_t[p], 16 * NB)
                if t.c >= L1 + 2:
                    step_wait(sp, st_o[p], t.pair(-L1, 16))
                sp.dma_start(x1[:, p, :], strip(t_dram, t, L1)).then_inc(ld_t[p], 16)

            def load_lx(s):
                back = L1 if s.c < L1 + NB else L1 + NB
                sp.dma_start(lx[:, :], strip(at_dram, s, back)[:, N:N + P]).then_inc(ld_lx, 16)

            def load_g2(s):
                step_wait(sp, st_g, s.of(16, 16 * (1 - L1)))
                sp.dma_start(g2[:, :], strip(g_dram, s, L1)[:, W:2 * W]).then_inc(ld_g2, 16)

            def store_out(t):
                step_wait(sp, o_ok, t.of(1, -L1))
                if t.c <= L1 + NB:
                    dst = ov[0, bass.ds(t.of(1, -L1 - 1), 1)]
                else:
                    dst = ov[1, bass.ds(t.of(1, -L1 - NB - 1), 1)]
                pp = (t.c - 1) % 2
                sp.dma_start(dst.rearrange("o p b f -> (o p) b f"), blocks(x1[:, pp, :])).then_inc(st_o[pp], 16)

            run_steps(sp, body)
            store_out(Step(None, LAST))
            for p in range(2):
                sp.wait_ge(st_o[p], 16 * NB)
                sp.wait_ge(st_t[p], 16 * NB)
                sp.wait_ge(st_at[p], 16 * NB // 2)
            sp.wait_ge(st_g, 16 * L1)
            for q in range(NQ):
                sp.wait_ge(st_s[q], 16 * NB)

        @block.tensor
        def _(pe):
            mm = nc.tensor.matmul
            pe.wait_ge(ident_ok, 2)
            pe.wait_ge(const0, 3)
            pe.wait_ge(d_zero, 2)

            def row_sums(n):
                k, g = CH0[n]
                pe.wait_ge(p0R, n + 1)
                last = None
                for j in range(4 * g, min(4 * g + 4, k)):
                    last = mm(psD[:, j, k:k + 1], sring[:, n % 4, (j - 4 * g) * P:(j - 4 * g + 1) * P], ones[:, :],
                              start=True, stop=True)
                (last if last is not None else nc.tensor.nop()).then_inc(p0D, 1)

            def rows_T(s, q):
                wait(pe, ld_r[q], s.of(16, 16))
                wait(pe, at_ok, s.of(4, q - 1))
                for j in range(4):
                    last = nc.tensor.transpose(psA[:, q % 2, j * P:(j + 1) * P], R[:, q, j * P:(j + 1) * P], ident[:, :])
                last.then_inc(rT, 1)

            for n, (k, g) in enumerate(CH0):
                if (k, g) == (NB - 1, 0):
                    for q in range(NQ):
                        if q < 2:
                            pe.wait_ge(p0S, n - 1 + q)
                        rows_T(Step(None, 0), q)
                    pe.wait_ge(at_ok, NQ)
                if g == 0:
                    pe.wait_ge(ld_row[k % 3], 16 * (k // 3 + 1))
                    if k:
                        pe.wait_ge(ld_col[k % 3], 16 * (k // 3 + (1 if k % 3 else 0)))
                if n >= 2:
                    pe.wait_ge(p0S, n - 1)
                for j in range(4 * g, min(4 * g + 4, k + 1)):
                    src = rowb[:, k % 3, j * P:(j + 1) * P] if j == k else colb[:, k % 3, j * P:(j + 1) * P]
                    last = nc.tensor.transpose(psA[:, n % 2, (j - 4 * g) * P:(j - 4 * g + 1) * P], src, ident[:, :])
                last.then_inc(p0T, 1)
                if n >= 2:
                    row_sums(n - 2)
            row_sums(len(CH0) - 2)
            row_sums(len(CH0) - 1)

            def turn(src, sem):
                for b in range(HB):
                    last = nc.tensor.transpose(psZ[:, b * F:(b + 1) * F], src[:, b * F:(b + 1) * F], ident[:, :])
                last.then_inc(sem, 1)

            def finish(t, k):
                c = t.c
                if k == 3 and 1 <= c <= L1:
                    wait(pe, z_ok, t.of(1, 0))
                    wait(pe, hThi, t.of(1, -2))
                    wait(pe, hTlo, t.of(1, -2))
                    turn(z, zT)
                if k == 7 and 1 <= c <= L1:
                    if c == 1:
                        pe.wait_ge(wlo_ok, 1)
                        pe.wait_ge(d_ok, 1)
                    wait(pe, zThi, t.of(1, 0))
                    wait(pe, zTlo, t.of(1, 0))
                    wait(pe, r1_ok, t.of(1, -1))
                    for b in range(HB):
                        f = slice(b * F, (b + 1) * F)
                        mm(psW[:, f], zTh[:, f], Wh[:, 0:F], start=True, stop=False)
                        mm(psW[:, f], zTh[:, f], Wl[:, 0:F], start=False, stop=False)
                        last = mm(psW[:, f], zTl[:, f], Wh[:, 0:F], start=False, stop=True)
                    last.then_inc(w_ok, 1)
                if k == 7 and 2 <= c < L1 + 2:
                    wait(pe, h2_ok, t.of(1, -1))
                    if c == L1 + 1:
                        wait(pe, zThi, t.of(1, -1))
                        wait(pe, zTlo, t.of(1, -1))
                    turn(h2, hT)
                if k in (11, 14) and 2 <= c < L1 + 2:
                    if k == 11:
                        wait(pe, hThi, t.of(1, -1))
                        wait(pe, hTlo, t.of(1, -1))
                    for b in ((0, 1) if k == 11 else (2, 3)):
                        f = slice(b * F, (b + 1) * F)
                        wait(pe, gev, t.of(4, -8 + b - 1))
                        mm(psG[:, b % 2, 0:3 * F], hTh[:, f], Wh[:, F:4 * F], start=True, stop=False)
                        mm(psG[:, b % 2, 0:3 * F], hTh[:, f], Wl[:, F:4 * F], start=False, stop=False)
                        mm(psG[:, b % 2, 0:3 * F], hTl[:, f], Wh[:, F:4 * F], start=False, stop=True).then_inc(g_ok, 1)

            def body(t):
                c = t.c
                rh, rl = half_of(c)
                acc = psAcc[:, c % 2, :]
                if 2 <= c < L1 + 2:
                    wait(pe, z_ok, t.of(1, -1))
                elif c >= L1 + 2:
                    wait(pe, o_ok, t.of(1, -1 - L1))
                if c > L1 and c != L1 + NB:
                    wait(pe, slot_hi, t.of(1, -L1))
                    wait(pe, slot_lo, t.of(1, -L1))
                for q in range(NQ):
                    wait(pe, lhi, t.of(4, q + 1))
                    wait(pe, llo, t.of(4, q + 1))
                    for j in range(4):
                        k = 4 * q + j
                        lh, ll = Lh[:, q, j * P:(j + 1) * P], Ll[:, q, j * P:(j + 1) * P]
                        if c % NB == 0:
                            pe.wait_ge(prep_hi, c + k + 1)
                            pe.wait_ge(prep_lo, c + k + 1)
                        mm(acc, lh, rh[:, k, :], start=k == 0, stop=False)
                        mm(acc, lh, rl[:, k, :], start=False, stop=False)
                        mm(acc, ll, rh[:, k, :], start=False, stop=c < L1 and k == NB - 1).then_inc(used, 1)
                        finish(t, k)
                    if c < NB - 1:
                        rows_T(Step(t.i, c + 1), q)
                if c >= L1:
                    wait(pe, lxh_ok, t.of(1, 1 - L1))
                    wait(pe, lxl_ok, t.of(1, 1 - L1))
                    wait(pe, g2h_ok, t.of(1, 1 - L1))
                    wait(pe, g2l_ok, t.of(1, 1 - L1))
                    mm(acc, lxh[:, :], g2h[:, :], start=False, stop=False)
                    mm(acc, lxh[:, :], g2l[:, :], start=False, stop=False)
                    mm(acc, lxl[:, :], g2h[:, :], start=False, stop=True).then_inc(acc1, 1)

            run_steps(pe, body)

        @block.scalar
        def _(act):
            A = nc.scalar.activation
            act.wait_ge(ld_w, 32)
            A(Wh[:, :], x1[:, 0, :], ACT.Copy).then_inc(whi_ok, 1)
            act.wait_ge(const0, 3)

            def h0(n):
                act.wait_ge(s0_nm, n + 1)
                n0 = n0s[n % 2]
                for b in range(HB):
                    f = slice(b * F, (b + 1) * F)
                    last = A(hst[:, n, f], hst[:, n, f], ACT.Relu, bias=n0.nm[:, b:b + 1], scale=n0.rs[:, b:b + 1])
                last.then_inc(s0_h, 1)

            def copy_T(s, q):
                wait(act, rT, s.of(4, q + 1))
                if q == 0:
                    wait(act, st_at[s.c % 2], s.pair(0, 16))
                A(AT[:, s.c % 2, q * Q:(q + 1) * Q], psA[:, q % 2, :], ACT.Copy).then_inc(at_ok, 1)

            def split_hi(s, q):
                if s.c < NB:
                    wait(act, S_ok, s.of(4, q + 1))
                else:
                    wait(act, ld_c[q], s.of(16, 16))
                if s.c:
                    wait(act, used, s.of(16, -16 + 4 * q + 4))
                A(Lh[:, q, :], C[:, q, :], ACT.Relu if s.c < L1 else ACT.Copy).then_inc(lhi, 1)

            for n, (k, g) in enumerate(CH0):
                if (k, g) == (NB - 1, 0):
                    for q in range(NQ):
                        copy_T(Step(None, 0), q)
                    for q in range(NQ):
                        split_hi(Step(None, 0), q)
                w = min(4, k + 1 - 4 * g) * P
                act.wait_ge(p0S, n + 1)
                A(sring[:, n % 4, 0:w], sring[:, n % 4, 0:w], ACT.Relu, accum_out=drow[:, k, g:g + 1]).then_inc(p0R, 1)
                if g == k // 4 and k:
                    h0(k - 1)
            h0(NB - 1)
            act.wait_ge(d_inv, 1)
            for n in range(NB):
                act.wait_ge(s0_h, n + 1)
                A(Xh[:, n, :], hst[:, n, :], ACT.Relu, scale=scal[:, 0, n:n + 1]).then_inc(prep_hi, 1)

            def gev_out(t, b):
                wait(act, tev, t.of(4, -8 + b + 1))
                if b == 0:
                    wait(act, st_g, t.of(16, -32))
                A(g12[:, :, b * F:(b + 1) * F],
                  psG[:, b % 2, F:3 * F].rearrange("p (k f) -> p k f", k=2), ACT.Copy).then_inc(gev, 1)

            def body(t):
                c = t.c
                pe_ = (c - 1) % 2
                nxt = Step(t.i, c + 1)
                if c:
                    split_hi(t, NQ - 1)
                if c >= L1:
                    wait(act, ld_lx, t.of(16, 16 * (1 - L1)))
                    wait(act, acc1, t.of(1, -L1))
                    A(lxh[:, :], lx[:, :], ACT.Copy).then_inc(lxh_ok, 1)
                    wait(act, ld_g2, t.of(16, 16 * (1 - L1)))
                    wait(act, slot_hi, t.of(1, -L1))
                    A(g2h[:, :], g2[:, :], ACT.Copy).then_inc(g2h_ok, 1)
                if 1 <= c <= L1:
                    wait(act, zT, t.of(1, 0))
                    wait(act, w_ok, t.of(1, -1))
                    A(zTh[:, :], psZ[:, :], ACT.Copy).then_inc(zThi, 1)
                if c < NB - 1:
                    copy_T(nxt, 0)
                if c < LAST - 1:
                    split_hi(nxt, 0)
                if c < L1 + NB:
                    prep(t)
                if 1 <= c <= L1:
                    wait(act, w_ok, t.of(1, 0))
                    wait(act, cur_ok, t.of(1, 1))
                    if c >= 3:
                        wait(act, st_t[pe_], t.pair(-1, 16))
                    elif c == 1:
                        act.wait_ge(wlo_ok, 1)
                    A(x1[:, pe_, :], psW[:, :], ACT.Relu, scale=cur_e[:, 2:3]).then_inc(r1_ok, 1)
                if 2 <= c < L1 + 2:
                    wait(act, hT, t.of(1, -1))
                    wait(act, g_ok, t.of(4, -8))
                    A(hTh[:, :], psZ[:, :], ACT.Copy).then_inc(hThi, 1)
                if c < NB - 1:
                    copy_T(nxt, 1)
                if c < LAST - 1:
                    split_hi(nxt, 1)
                if c < NB - 1:
                    copy_T(nxt, 2)
                if 2 <= c < L1 + 2:
                    gev_out(t, 0)
                    gev_out(t, 1)
                if c < LAST - 1:
                    split_hi(nxt, 2)
                if 1 <= c <= L1:
                    wait(act, e_nm, t.of(1, 0))
                    wait(act, hT, t.of(1, -1))
                    for b in range(HB):
                        f = slice(b * F, (b + 1) * F)
                        last = A(h2[:, f], x1[:, pe_, f], ACT.Relu, bias=ne.nm[:, b:b + 1], scale=ne.rs[:, b:b + 1])
                    last.then_inc(h2_ok, 1)
                if 2 <= c < L1 + 2:
                    gev_out(t, 2)
                    gev_out(t, 3)
                if c >= L1:
                    slot(t)
                if c < NB - 1:
                    copy_T(nxt, 3)

            def prep(t):
                c = t.c
                dst, _ = half_of(c + NB)
                if c < NB:
                    wait(act, p_nm, t.of(1, 1))
                    for b in range(HB):
                        f = slice(b * F, (b + 1) * F)
                        last = A(xp[:, f], xp[:, f], ACT.Relu, bias=npn.nm[:, b:b + 1], scale=npn.rs[:, b:b + 1])
                    last.then_inc(p_h, 1)
                    wait(act, p_h, t.of(1, 1))
                    off = t.of(1, 0)
                else:
                    wait(act, ld_xp, t.of(16, 16))
                    act.wait_ge(used, NB * (c // NB) * NB)
                    wait(act, hsum, t.of(1, 1 - NB))
                    off = t.of(1, -(c // NB) * NB)
                A(dst[:, bass.ds(off, 1), :], xp[:, :].rearrange("p (o w) -> p o w", o=1), ACT.Copy).then_inc(prep_hi, 1)

            def slot(t):
                dst, _ = half_of(t.c)
                back = L1 if t.c < L1 + NB else L1 + NB
                wait(act, used, t.of(17, 1 - back))
                wait(act, g2h_ok, t.of(1, 1 - L1))
                A(dst[:, bass.ds(t.of(1, -back), 1), :], g2h[:, :].bitcast(F32).rearrange("p (o w) -> p o w", o=1),
                  ACT.Copy).then_inc(slot_hi, 1)

            run_steps(act, body)

        @block.vector
        def _(dve):
            V = nc.vector

            def stats(nrm, src, st, mv, ve, seen):
                for b in range(HB):
                    last = V.bn_stats(nrm.st[:, b, :], src[:, b * F:(b + 1) * F])
                last.then_inc(st, 1)
                step_wait(dve, st, seen)
                for b in range(HB):
                    last = V.bn_aggr(nrm.mv[:, b, :], nrm.st[:, b, :])
                last.then_inc(mv, 1)
                wait(dve, mv, seen)
                V.tensor_scalar(nrm.ve[:, :], nrm.mv[:, :, 1], EPS, None, ALU.add).then_inc(ve, 1)

            def neg_mean(nrm, sem):
                V.scalar_tensor_tensor(out=nrm.nm[:, :], in0=nrm.mv[:, :, 0], scalar=-1.0, in1=nrm.rs[:, :],
                                       op0=ALU.mult, op1=ALU.mult).then_inc(sem, 1)

            def sum_T(s, q):
                wait(dve, at_ok, s.of(4, q + 1))
                wait(dve, ld_c[q], s.of(16, 16))
                V.tensor_tensor(C[:, q, :], AT[:, s.c % 2, q * Q:(q + 1) * Q], C[:, q, :], ALU.add).then_inc(S_ok, 1)

            def split_lo(s, q):
                wait(dve, lhi, s.of(4, q + 1))
                if s.c < L1:
                    V.scalar_tensor_tensor(out=Ll[:, q, :], in0=C[:, q, :], scalar=0.0, in1=Lh[:, q, :].bitcast(F32),
                                           op0=ALU.max, op1=ALU.subtract).then_inc(llo, 1)
                else:
                    V.tensor_tensor(Ll[:, q, :], C[:, q, :], Lh[:, q, :].bitcast(F32), ALU.subtract).then_inc(llo, 1)

            V.memset(psD[:, :, :], 0.0).then_inc(d_zero, 1)
            V.memset(drow[:, :, :], 0.0).then_inc(d_zero, 1)
            V.memset(ones[:, :], 1.0).then_inc(const0, 1)
            dve.wait_ge(whi_ok, 1)
            V.tensor_tensor(Wl[:, :], x1[:, 0, :], Wh[:, :].bitcast(F32), ALU.subtract).then_inc(wlo_ok, 1)
            dve.wait_ge(d_zero, 2)
            def mean0(n):
                dve.wait_ge(s0_rs, n + 1)
                neg_mean(n0s[n % 2], s0_nm)

            for n, (k, g) in enumerate(CH0):
                if (k, g) == (NB - 1, 0):
                    for q in range(NQ):
                        sum_T(Step(None, 0), q)
                w = min(4, k + 1 - 4 * g) * P
                dve.wait_ge(p0T, n + 1)
                if n >= 4:
                    dve.wait_ge(p0D, n - 3)
                V.tensor_tensor(sring[:, n % 4, 0:w], psA[:, n % 2, 0:w], rowb[:, k % 3, 4 * g * P:4 * g * P + w],
                                ALU.add).then_inc(p0S, 1)
                if g == k // 4:
                    if k:
                        mean0(k - 1)
                    if k >= 2:
                        dve.wait_ge(s0_h, k - 1)
                    dve.wait_ge(ld_x0[k], 16)
                    stats(n0s[k % 2], hst[:, k, :], s0_st, s0_mv, s0_ve, k + 1)
            mean0(NB - 1)
            dve.wait_ge(p0D, len(CH0))
            V.reduce_sum(d1[:, :], psD[:, :, :], axis=AX.X).then_inc(d_sums, 1)
            dve.wait_ge(p0R, len(CH0))
            V.reduce_sum(d2[:, :], drow[:, :, :], axis=AX.X).then_inc(d_sums, 1)
            dve.wait_ge(d_sums, 2)
            V.tensor_tensor(d1[:, :], d1[:, :], d2[:, :], ALU.add).then_inc(d_sum, 1)
            dve.wait_ge(d_sum, 1)
            V.tensor_scalar(d2[:, :], d1[:, :], 0.0, None, ALU.is_le).then_inc(d_none, 1)
            dve.wait_ge(d_none, 1)
            V.scalar_tensor_tensor(out=dsafe[:, :], in0=d1[:, :], scalar=0.5, in1=d2[:, :],
                                   op0=ALU.mult, op1=ALU.add).then_inc(d_safe, 1)
            dve.wait_ge(d_inv, 1)
            V.scalar_tensor_tensor(out=scal[:, 1, :], in0=scal[:, 0, :], scalar=-0.5, in1=scal[:, 0, :],
                                   op0=ALU.mult, op1=ALU.mult).then_inc(d_ok, 1)

            for q in range(NQ):
                split_lo(Step(None, 0), q)
            for n in range(NB):
                dve.wait_ge(prep_hi, n + 1)
                V.scalar_tensor_tensor(out=Xl[:, n, :], in0=hst[:, n, :], scalar=scal[:, 0, n:n + 1],
                                       in1=Xh[:, n, :].bitcast(F32), op0=ALU.mult, op1=ALU.subtract).then_inc(prep_lo, 1)
            dve.wait_ge(ld_diag, 16)
            dve.wait_ge(d_sq, 1)
            dve.wait_ge(d_ok, 1)

            def pick(dst, t, shift):
                back = shift + NB * ((t.c - shift) // NB)
                o = t.of(1, -back)
                return V.tensor_copy(dst[:, :].rearrange("p (k o) -> p k o", o=1), scal[:, :, bass.ds(o, 1)])

            def t_out(t, b):
                f = slice(b * F, (b + 1) * F)
                wait(dve, g_ok, t.of(4, -8 + b + 1))
                V.scalar_tensor_tensor(out=x1[:, t.c % 2, f], in0=psG[:, b % 2, 0:F], scalar=cur_g[:, 3:4],
                                       in1=x1[:, t.c % 2, f], op0=ALU.mult, op1=ALU.add).then_inc(tev, 1)

            def body(t):
                c = t.c
                pe_ = (c - 1) % 2
                nxt = Step(t.i, c + 1)
                if c < L1 + 2:
                    picks = ([(cur_g, 2)] if c >= 2 else []) + ([(cur_p, 0)] if c < NB else []) \
                        + ([(cur_e, 1)] if 1 <= c <= L1 else [])
                    for dst, shift in picks:
                        last = pick(dst, t, shift)
                    last.then_inc(cur_ok, 1)
                    wait(dve, cur_ok, t.of(1, 1))
                if 1 <= c <= L1:
                    wait(dve, hsum, t.of(1, 0))
                    wait(dve, used, t.of(16, 0))
                    V.scalar_tensor_tensor(out=z[:, :], in0=psAcc[:, pe_, :], scalar=cur_e[:, 1:2], in1=z[:, :],
                                           op0=ALU.mult, op1=ALU.add).then_inc(z_ok, 1)
                if c > L1:
                    result(t)
                if 1 <= c < NB:
                    sum_T(t, NQ - 1)
                if c < NB:
                    wait(dve, ld_xp, t.of(16, 16))
                    stats(npn, xp, p_st, p_mv, p_ve, t.of(1, 1))
                if c:
                    split_lo(t, NQ - 1)
                if c >= L1:
                    wait(dve, lxh_ok, t.of(1, 1 - L1))
                    V.tensor_tensor(lxl[:, :], lx[:, :], lxh[:, :].bitcast(F32), ALU.subtract).then_inc(lxl_ok, 1)
                    wait(dve, g2h_ok, t.of(1, 1 - L1))
                    wait(dve, slot_lo, t.of(1, -L1))
                    V.tensor_tensor(g2l[:, :], g2[:, :], g2h[:, :].bitcast(F32), ALU.subtract).then_inc(g2l_ok, 1)
                if 1 <= c <= L1:
                    wait(dve, zThi, t.of(1, 0))
                    V.tensor_tensor(zTl[:, :], psZ[:, :], zTh[:, :].bitcast(F32), ALU.subtract).then_inc(zTlo, 1)
                if c < NB:
                    wait(dve, p_rs, t.of(1, 1))
                    V.tensor_scalar(npn.rs[:, :], npn.rs[:, :], cur_p[:, 0:1], None, ALU.mult).then_inc(p_sc, 1)
                    if c < NB - 1:
                        sum_T(nxt, 0)
                    wait(dve, p_sc, t.of(1, 1))
                    neg_mean(npn, p_nm)
                if c < LAST - 1:
                    split_lo(nxt, 0)
                if 1 <= c <= L1:
                    wait(dve, r1_ok, t.of(1, 0))
                    wait(dve, ld_xe, t.of(16, 0))
                    V.tensor_tensor(x1[:, pe_, :], x1[:, pe_, :], xe[:, :], ALU.add).then_inc(x1_ok, 1)
                if 2 <= c < L1 + 2:
                    wait(dve, hThi, t.of(1, -1))
                    V.tensor_tensor(hTl[:, :], psZ[:, :], hTh[:, :].bitcast(F32), ALU.subtract).then_inc(hTlo, 1)
                if c < NB - 1:
                    sum_T(nxt, 1)
                if 1 <= c <= L1:
                    wait(dve, x1_ok, t.of(1, 0))
                    stats(ne, x1[:, pe_, :], e_st, e_mv, e_ve, t.of(1, 0))
                if c < LAST - 1:
                    split_lo(nxt, 1)
                if 2 <= c < L1 + 2:
                    wait(dve, xb_ok, t.of(1, -1))
                    t_out(t, 0)
                    t_out(t, 1)
                if c < NB - 1:
                    sum_T(nxt, 2)
                if 1 <= c <= L1:
                    wait(dve, e_rs, t.of(1, 0))
                    neg_mean(ne, e_nm)
                if 2 <= c < L1 + 2:
                    t_out(t, 2)
                    t_out(t, 3)
                    wait(dve, tev, t.of(4, -4))
                if c < LAST - 1:
                    split_lo(nxt, 2)
                if c >= L1:
                    slot(t)

            def slot(t):
                _, dst = half_of(t.c)
                back = L1 if t.c < L1 + NB else L1 + NB
                wait(dve, used, t.of(17, 1 - back))
                wait(dve, g2l_ok, t.of(1, 1 - L1))
                V.tensor_copy(dst[:, bass.ds(t.of(1, -back), 1), :],
                              g2l[:, :].bitcast(F32).rearrange("p (o w) -> p o w", o=1)).then_inc(slot_lo, 1)

            def result(t):
                pp = (t.c - 1) % 2
                wait(dve, acc1, t.of(1, -L1))
                wait(dve, ld_t[pp], t.pair(-1 - L1, 16) + 16)
                V.tensor_tensor(x1[:, pp, :], psAcc[:, pp, :], x1[:, pp, :], ALU.add).then_inc(o_ok, 1)

            run_steps(dve, body)
            result(Step(None, LAST))

        @block.gpsimd
        def _(pool):
            G = nc.gpsimd
            G.memset(mhalf[:, :], -0.5).then_inc(const0, 1)
            G.memset(half[:, :], 0.5).then_inc(const0, 1)
            G.memset(ident[:, :], 0.0).then_inc(ident_ok, 1)
            pool.wait_ge(ident_ok, 1)
            G.affine_select(out=ident[:, :], in_=ident[:, :], compare_op=ALU.not_equal, fill=1.0,
                            base=0, pattern=[[-1, P]], channel_multiplier=1).then_inc(ident_ok, 1)
            pool.wait_ge(const0, 3)

            def power(out, base, exponent):
                return G.tensor_tensor(out=out, in0=base, in1=exponent, op=ALU.pow)

            for n in range(NB):
                pool.wait_ge(s0_ve, n + 1)
                power(n0s[n % 2].rs[:, :], n0s[n % 2].ve[:, :], mhalf[:, 0:HB]).then_inc(s0_rs, 1)
            pool.wait_ge(d_safe, 1)
            power(scal[:, 0, :], dsafe[:, :], mhalf[:, :]).then_inc(d_inv, 1)
            power(scal[:, 2, :], dsafe[:, :], half[:, :]).then_inc(d_sq, 1)

            def masks(s):
                p = s.c % 2
                wait(pool, S_ok, s.of(4, 4))
                at = AT[:, p, :].rearrange("p (j c) -> p j c", c=P)
                if not isinstance(s.of(1, 0), int) or s.c:
                    step_wait(pool, mk_ok, s.of(1, 0))
                G.tensor_copy(dmid[:, :].rearrange("p (o c) -> p o c", o=1), at[:, bass.ds(s.of(1, 0), 1), :]).then_inc(mk_c, 1)
                wait(pool, mk_c, s.of(1, 1))
                G.tensor_tensor(out=tiny[:, :], in0=half[:, 0:1], in1=half[:, 0:1], op=ALU.add)
                G.affine_select(out=AT[:, p, N:N + P], in_=dmid[:, :], compare_op=ALU.is_gt, fill=0.0,
                                base=0, pattern=[[1, P]], channel_multiplier=-1)
                G.affine_select(out=dmid[:, :], in_=dmid[:, :], compare_op=ALU.is_gt, fill=0.0,
                                base=0, pattern=[[-1, P]], channel_multiplier=1).then_inc(mk_s, 1)
                step_wait(pool, mk_s, s.of(1, 1))
                G.tensor_copy(at[:, bass.ds(s.of(1, 0), 1), :], dmid[:, :].rearrange("p (o c) -> p o c", o=1)).then_inc(mk_ok, 1)

            pool.wait_ge(ld_bias, 16)

            def body(t):
                c = t.c
                pe_ = (c - 1) % 2
                if c < NB:
                    masks(t)
                    wait(pool, p_ve, t.of(1, 1))
                    power(npn.rs[:, :], npn.ve[:, :], mhalf[:, 0:HB]).then_inc(p_rs, 1)
                if c < L1:
                    hi, lo = half_of(c)
                    o = t.of(1, -NB * (c // NB))
                    pool.wait_ge(prep_hi, NB * (c // NB + 1))
                    pool.wait_ge(prep_lo, NB * (c // NB + 1))
                    wait(pool, zT, t.of(1, 0))
                    G.tensor_tensor(out=z[:, :].rearrange("p (o w) -> p o w", o=1), in0=hi[:, bass.ds(o, 1), :].bitcast(F32),
                                    in1=lo[:, bass.ds(o, 1), :].bitcast(F32), op=ALU.add).then_inc(hsum, 1)
                if c < L1 + NB:
                    hi, lo = half_of(c + NB)
                    wait(pool, prep_hi, t.of(1, NB + 1))
                    o = t.of(1, -(c // NB) * NB)
                    G.tensor_tensor(out=lo[:, bass.ds(o, 1), :], in0=xp[:, :].rearrange("p (o w) -> p o w", o=1),
                                    in1=hi[:, bass.ds(o, 1), :].bitcast(F32), op=ALU.subtract).then_inc(prep_lo, 1)
                if 1 <= c <= L1:
                    wait(pool, e_ve, t.of(1, 0))
                    power(ne.rs[:, :], ne.ve[:, :], mhalf[:, 0:HB]).then_inc(e_rs, 1)
                    wait(pool, h2_ok, t.of(1, 0))
                    G.tensor_tensor(out=blocks(x1[:, pe_, :]), in0=blocks(x1[:, pe_, :]),
                                    in1=biasb[:, :].unsqueeze(1).to_broadcast([P, HB, F]), op=ALU.add).then_inc(xb_ok, 1)

            for c in (0, 1, 2, 3):
                body(Step(None, c))
            with pool.Fori(0, 5) as i:
                for c in (4, 5):
                    body(Step(i, c))
            for c in (14, 15, 16, 17):
                body(Step(None, c))
            with pool.Fori(0, 6) as i:
                for c in (18, 19):
                    body(Step(i, c))
            for c in (30, 31, 32, 33):
                body(Step(None, c))
            with pool.Fori(0, 6) as i:
                for c in (34, 35):
                    body(Step(i, c))
            for c in (46, 47):
                body(Step(None, c))


_INS = ["x", "adj", "L0_gnn_W", "L1_gnn_W", "L1_gnn_bias"]


def kernel(**inputs):
    import numpy as _np
    import concourse.bacc as _bacc
    from concourse import mybir as _mybir
    from concourse.bass_utils import run_bass_kernel_spmd as _run

    nc = _bacc.Bacc("TRN2", target_bir_lowering=False, num_devices=1)
    arrays, args = {}, []
    for name in _INS:
        a = _np.ascontiguousarray(inputs[name])
        arrays[f"in_{name}"] = a
        args.append(nc.dram_tensor(f"in_{name}", a.shape, _mybir.dt.from_np(a.dtype), kind="ExternalInput").ap())
    args.append(nc.dram_tensor("result", (B, N, F), _mybir.dt.float32, kind="ExternalOutput").ap())
    build(nc, *args)
    r = _run(nc, [arrays], core_ids=[0])
    return r.results[0]["result"]
```
